# Optimizing a Trainium2 kernel written in Bass

```python
import numpy as np
import jax
import jax.numpy as jnp

def _softmax(x, axis=-1):
    return jax.nn.softmax(x, axis=axis)

def _gelu(x):
    return jax.nn.gelu(x, approximate=True)

def _silu(x):
    return jax.nn.silu(x)

def _sigmoid(x):
    return jax.nn.sigmoid(x)

def _layernorm(x, axis=-1, eps=1e-05):
    m = jnp.mean(x, axis=axis, keepdims=True)
    v = jnp.var(x, axis=axis, keepdims=True)
    return (x - m) / jnp.sqrt(v + eps)

def _scatter_add(tgt, idx, src, axis=0):
    return tgt.at[idx].add(src)

def _segment_sum(src, seg, n):
    return jax.ops.segment_sum(src, seg, n)
kernel_name = 'mk_gnn_preln_d2_gnn_r32_71ac7e'

def setup_inputs(seed: int=0):
    np.random.seed(seed)
    _w = jnp.asarray

    def _rec_inputs():
        import jax
        import jax.numpy as jnp
        _gk = jax.random.key(seed)
        x = -0.000202 + 1 * jax.random.normal(jax.random.fold_in(_gk, 1), (3125, 128), jnp.float32)
        _s = jax.random.randint(jax.random.fold_in(_gk, 2), (25000,), 0, 3125, jnp.int32)
        _d = jax.random.randint(jax.random.fold_in(_gk, 3), (25000,), 0, 3125, jnp.int32)
        _loop = jnp.arange(3125, dtype=jnp.int32)
        src = jnp.concatenate([_s, _d, _loop])
        dst = jnp.concatenate([_d, _s, _loop])
        _o = jnp.argsort(dst, stable=True)
        src = src[_o]
        dst = dst[_o]
        edge_attr_128 = 5.93493e-05 + 1.00006 * jax.random.normal(jax.random.fold_in(_gk, 11), (53125, 128), jnp.float32)
        return (x, src, dst, edge_attr_128)
    x, src, dst, edge_attr_128 = _rec_inputs()

    def _L0_gnn_setup():
        import jax, jax.numpy as jnp
        import numpy as np
        N_NODES = 50000

        def sage_conv(x, src, dst, Wl, bl, Wr, n_nodes):
            msg = x[src]
            summed = jax.ops.segment_sum(msg, dst, num_segments=n_nodes)
            ones = jnp.ones((src.shape[0], 1), dtype=x.dtype)
            cnt = jax.ops.segment_sum(ones, dst, num_segments=n_nodes)
            agg = summed / jnp.maximum(cnt, 1.0)
            return agg @ Wl.T + bl + x @ Wr.T
        key = jax.random.key(seed)
        ks = jax.random.split(key, 12)
        d = 128
        E = 25000
        x = jax.random.normal(ks[0], (N_NODES, d), dtype=jnp.float32)
        edge_index = jax.random.randint(ks[1], (2, E), 0, N_NODES, dtype=jnp.int64)
        s = 0.05
        mk = lambda k: jax.random.normal(k, (d, d), dtype=jnp.float32) * s
        return {'x': x, 'edge_index': edge_index, 'W1l': mk(ks[2]), 'b1': jnp.zeros((d,), jnp.float32), 'W1r': mk(ks[3]), 'W2l': mk(ks[4]), 'b2': jnp.zeros((d,), jnp.float32), 'W2r': mk(ks[5]), 'W3l': mk(ks[6]), 'b3': jnp.zeros((d,), jnp.float32), 'W3r': mk(ks[7])}
    _L0_gnn_all = _L0_gnn_setup()
    _L0_gnn_in = {k: v for k, v in _L0_gnn_all.items() if k in ('W1l', 'b1', 'W1r', 'W2l', 'b2', 'W2r', 'W3l', 'b3', 'W3r')}
    del _L0_gnn_all

    def _L1_gnn_setup():
        import jax, jax.numpy as jnp
        import numpy as np
        N = 50000
        E = 18750
        D = 128

        def _mlp(x, W1, b1, W2, b2):
            h = jax.nn.gelu(x @ W1 + b1, approximate=False)
            return h @ W2 + b2
        key = jax.random.key(seed)
        ks = jax.random.split(key, 12)
        s = 1.0 / np.sqrt(D)
        inp = {'x': jax.random.normal(ks[0], (N, D), dtype=jnp.float32), 'edge_index': jax.random.randint(ks[1], (2, E), 0, N, dtype=jnp.int64), 'edge_attr': jax.random.normal(ks[2], (E, D), dtype=jnp.float32), 'We1': jax.random.uniform(ks[3], (D, D), jnp.float32, -s, s), 'be1': jax.random.uniform(ks[4], (D,), jnp.float32, -s, s), 'We2': jax.random.uniform(ks[5], (D, D), jnp.float32, -s, s), 'be2': jax.random.uniform(ks[6], (D,), jnp.float32, -s, s), 'Wu1': jax.random.uniform(ks[7], (D, D), jnp.float32, -s, s), 'bu1': jax.random.uniform(ks[8], (D,), jnp.float32, -s, s), 'Wu2': jax.random.uniform(ks[9], (D, D), jnp.float32, -s, s), 'bu2': jax.random.uniform(ks[10], (D,), jnp.float32, -s, s), 'eps': jnp.zeros((1,), dtype=jnp.float32)}
        return inp
    _L1_gnn_all = _L1_gnn_setup()
    _L1_gnn_in = {k: v for k, v in _L1_gnn_all.items() if k in ('We1', 'be1', 'We2', 'be2', 'Wu1', 'bu1', 'Wu2', 'bu2', 'eps')}
    del _L1_gnn_all
    return {'x': x, 'src': src, 'dst': dst, 'edge_attr_128': edge_attr_128, 'L0_gnn_W1l': _L0_gnn_in['W1l'], 'L0_gnn_b1': _L0_gnn_in['b1'], 'L0_gnn_W1r': _L0_gnn_in['W1r'], 'L0_gnn_W2l': _L0_gnn_in['W2l'], 'L0_gnn_b2': _L0_gnn_in['b2'], 'L0_gnn_W2r': _L0_gnn_in['W2r'], 'L0_gnn_W3l': _L0_gnn_in['W3l'], 'L0_gnn_b3': _L0_gnn_in['b3'], 'L0_gnn_W3r': _L0_gnn_in['W3r'], 'L1_gnn_We1': _L1_gnn_in['We1'], 'L1_gnn_be1': _L1_gnn_in['be1'], 'L1_gnn_We2': _L1_gnn_in['We2'], 'L1_gnn_be2': _L1_gnn_in['be2'], 'L1_gnn_Wu1': _L1_gnn_in['Wu1'], 'L1_gnn_bu1': _L1_gnn_in['bu1'], 'L1_gnn_Wu2': _L1_gnn_in['Wu2'], 'L1_gnn_bu2': _L1_gnn_in['bu2'], 'L1_gnn_eps': _L1_gnn_in['eps']}

def reference(x, src, dst, edge_attr_128, L0_gnn_W1l, L0_gnn_b1, L0_gnn_W1r, L0_gnn_W2l, L0_gnn_b2, L0_gnn_W2r, L0_gnn_W3l, L0_gnn_b3, L0_gnn_W3r, L1_gnn_We1, L1_gnn_be1, L1_gnn_We2, L1_gnn_be2, L1_gnn_Wu1, L1_gnn_bu1, L1_gnn_Wu2, L1_gnn_bu2, L1_gnn_eps):
    import jax
    import jax.numpy as jnp

    def _L0_gnn_ref(x, edge_index, W1l, b1, W1r, W2l, b2, W2r, W3l, b3, W3r):
        import jax, jax.numpy as jnp
        import numpy as np
        N_NODES = 50000

        def sage_conv(x, src, dst, Wl, bl, Wr, n_nodes):
            msg = x[src]
            summed = jax.ops.segment_sum(msg, dst, num_segments=n_nodes)
            ones = jnp.ones((src.shape[0], 1), dtype=x.dtype)
            cnt = jax.ops.segment_sum(ones, dst, num_segments=n_nodes)
            agg = summed / jnp.maximum(cnt, 1.0)
            return agg @ Wl.T + bl + x @ Wr.T
        src, dst = (edge_index[0], edge_index[1])
        n = x.shape[0]
        h = jax.nn.relu(sage_conv(x, src, dst, W1l, b1, W1r, n))
        h = jax.nn.relu(sage_conv(h, src, dst, W2l, b2, W2r, n))
        return sage_conv(h, src, dst, W3l, b3, W3r, n)

    def _L1_gnn_ref(x, edge_index, edge_attr, We1, be1, We2, be2, Wu1, bu1, Wu2, bu2, eps):
        import jax, jax.numpy as jnp
        import numpy as np
        N = 50000
        E = 18750
        D = 128

        def _mlp(x, W1, b1, W2, b2):
            h = jax.nn.gelu(x @ W1 + b1, approximate=False)
            return h @ W2 + b2
        src, dst = (edge_index[0], edge_index[1])
        messages = _mlp(x[src] + edge_attr, We1, be1, We2, be2)
        aggregated = jax.ops.segment_sum(messages, dst, num_segments=x.shape[0])
        return _mlp((1.0 + eps) * x + aggregated, Wu1, bu1, Wu2, bu2)
    edge_index = jnp.stack([src, dst])
    h = jnp.maximum(_layernorm(x, axis=-1), 0.0)
    x = x + _L0_gnn_ref(h, edge_index, L0_gnn_W1l, L0_gnn_b1, L0_gnn_W1r, L0_gnn_W2l, L0_gnn_b2, L0_gnn_W2r, L0_gnn_W3l, L0_gnn_b3, L0_gnn_W3r)
    h = jnp.maximum(_layernorm(x, axis=-1), 0.0)
    x = x + _L1_gnn_ref(h, edge_index, edge_attr_128, L1_gnn_We1, L1_gnn_be1, L1_gnn_We2, L1_gnn_be2, L1_gnn_Wu1, L1_gnn_bu1, L1_gnn_Wu2, L1_gnn_bu2, L1_gnn_eps)
    return x

_drawn_inputs = setup_inputs


def setup_inputs(seed=0):
    import zlib

    import numpy as np

    out = dict(_drawn_inputs(seed))
    spreads = {'L0_gnn_b1': (0.0, 0.371), 'L0_gnn_b2': (0.0, 0.1), 'L0_gnn_b3': (0.0, 0.1)}
    factors = {'L1_gnn_bu1': 2.963}
    for name, (base, spread) in spreads.items():
        noise = np.random.default_rng([zlib.crc32(name.encode()), seed]).standard_normal(out[name].shape)
        drawn = base * np.exp(spread * noise) if base else spread * noise
        out[name] = jnp.asarray(drawn.astype(out[name].dtype))
    for name, factor in factors.items():
        out[name] = (out[name] * factor).astype(out[name].dtype)
    return out
```

```python
from contextlib import ExitStack

import numpy as np

import concourse.bass as bass
from concourse import mybir

ALU = mybir.AluOpType
ACT = mybir.ActivationFunctionType
AX = mybir.AxisListType
F32 = mybir.dt.float32
BF16 = mybir.dt.bfloat16
I32 = mybir.dt.int32
F16 = mybir.dt.float16

P = 128
D = 128
BANK = 512
EPS_LN = 1e-5


class Shapes:

    def __init__(self, n_nodes, n_edges):
        self.N, self.E = n_nodes, n_edges
        self.NP = 125
        self.NB = n_nodes // self.NP
        self.EP = 125
        self.TG = 5
        self.NG = n_edges // (self.EP * self.TG)
        self.NT = self.NG * self.TG
        assert self.NP * self.NB == n_nodes and self.NT * self.EP == n_edges and self.NG % 2 == 1
        self.CH = -(-n_nodes // BANK)
        self.W = 128
        self.DT = 2
        self.DG = self.NT // self.DT
        self.DW = BANK // self.NB
        assert self.NT % self.DT == 1 and self.DG % 4 == 0


RING = 10
SB_RING = 5
PS_RING = 2


def semaphores(nc, ctx, prefix=""):
    taken = []

    def sem(name):
        taken.append(nc.alloc_semaphore(prefix + name))
        return taken[-1]

    def clear():
        nc.clear_and_free_semaphores(taken)
        nc.all_engine_barrier()
    ctx.callback(clear)
    return sem


def chunk(s, c):
    return min(BANK, s.N - c * BANK)


def gnn_kernel(nc, t, out):
    s = Shapes(t["x"].shape[0], t["src"].shape[0])
    table = nc.dram_tensor("table", (s.N, D), F32, kind="Internal").ap()
    counts = nc.dram_tensor("counts", (s.NB, s.N), F16, kind="Internal").ap()
    lists = {n: nc.dram_tensor("list_" + n, (P, s.NT + RING), dt, kind="Internal").ap()
             for n, dt in (("src_idx", I32), ("dst_abs", F32), ("dst_rel", F32))}
    engines = (nc.sync, nc.gpsimd, nc.scalar, nc.vector, nc.tensor)
    with ExitStack() as ctx:
        k = {}

        def tensors(ctx, **shapes):
            for name, (shape, dt) in shapes.items():
                again = "_2" if name in k else ""
                k[name] = ctx.enter_context(nc.sbuf_tensor(name + again, shape, dt))
        k["ps"] = ctx.enter_context(nc.psum_tensor("ps", [P, 8 * BANK], F32))
        tensors(ctx, ident=([P, P], F32), hn=([P, s.NB * D], F32), spill=([1, 1], I32), starts=([1, s.NG], I32),
                eps1=([P, 1], F32), ones=([P, P], F32),
                **{n: ([P, D], F32) for n in ("W1l", "W1r", "W2l", "W2r", "W3l", "W3r")},
                **{n: ([1, D], F32) for n in ("b1", "b2", "b3")})
        with ExitStack() as first:
            tensors(first, x=([P, s.NB * D], F32), iota=([P, BANK], F32), iota16=([P, BANK], F16),
                    zeros=([P, BANK], BF16), src_idx=([P, s.NT + RING], I32), dst_abs=([P, s.NT], F32),
                    dst_rel=([P, s.NT], F32))
            prepare(nc, s, t, k)
            save_lists(nc, s, k, lists)
            layer_norm(nc, s, k, "ln0")
        with ExitStack() as dense:
            tensors(dense, adj=([P, s.NB, s.N + s.DW], F16), rcnt=([P, s.NB], F32))
            with ExitStack() as keys:
                tensors(keys, key=([P, s.NT], F32), low=([P, s.NT], F32), dstarts=([1, s.DG + 1], I32),
                        next_key=([P, s.NT], F32))
                dense_keys(nc, s, t, k)
                spill = nc.values_load(k["spill"][0:1, 0:1], min_val=0, max_val=1)
                with nc.If(spill):
                    for e in engines:
                        e.nop()
                with nc.Else():
                    for e in engines:
                        e.nop()
                    build_adjacency(nc, s, k)
            with nc.If(spill):
                for e in engines:
                    e.nop()
            with nc.Else():
                for e in engines:
                    e.nop()
                dense_counts(nc, s, k, counts)
                dense_layers(nc, s, k)
        tensors(ctx, src_idx=([P, s.NT + RING], I32), dst_abs=([P, s.NT], F32), dst_rel=([P, s.NT], F32),
                iota=([P, BANK], F32), zeros=([P, BANK], BF16), cnt1=([1, s.N], F32), hT=([P, s.N], F32),
                aT=([P, s.N + s.W], F32), rcntT=([P, s.N], F32), x=([P, s.NB * D], F32),
                **{n: ([P, D], F32) for n in ("We1", "We2", "Wu1", "Wu2")},
                **{n: ([P, 1], F32) for n in ("b1c", "b2c", "b3c", "bu1")},
                **{n: ([1, D], F32) for n in ("be1", "be2", "bu2")})
        load_second(nc, s, t, k, lists)

        def edges(kind, name):
            for first in range(0, s.CH, 4):
                n = min(4, s.CH - first)
                zero_sums(nc, s, k, n)
                edge_pass(nc, s, t, k, table, kind, (first, n), f"{name}g{first}")
                take_sums(nc, s, k, first, n)

        with nc.If(spill):
            for e in engines:
                e.nop()
            edges("count", "cnt")
            take_counts(nc, s, k)
            turn_rows(nc, s, k, table, None, "turn0")
            for layer in (1, 2, 3):
                edges("sage", f"sage{layer}")
                sage_nodes(nc, s, k, table, layer)
        with nc.Else():
            for e in engines:
                e.nop()
            count_row(nc, s, k, counts)
        residual(nc, s, k)
        layer_norm(nc, s, k, "ln1")
        turn_rows(nc, s, k, table, "We1", "turn3")
        with nc.If(spill):
            for e in engines:
                e.nop()
            edges("gine", "gine")
        with nc.Else():
            for e in engines:
                e.nop()
            edge_pass(nc, s, t, k, table, "gine", None, "ginew")
        gine_nodes(nc, s, k, out)


def prepare(nc, s, t, k):
    with ExitStack() as ctx:
        def sb(name, shape, dt=F32):
            return ctx.enter_context(nc.sbuf_tensor(name, shape, dt))

        sem = semaphores(nc, ctx)
        raw = {n: sb(n + "_raw", [P, D]) for n in ("W1l", "W1r", "W2l", "W2r", "W3l", "W3r")}
        ed = {n: sb(n + "_raw", [P, s.EP * s.TG], I32) for n in ("src", "dst")}
        srcf = sb("srcf", [P, s.EP * s.TG])
        dstf = sb("dstf", [P, s.EP * s.TG])
        relf = sb("relf", [P, s.EP * s.TG])
        col = sb("col", [P, 4])
        epst = sb("epst", [1, 1])
        viol = sb("viol", [1, 1])
        iota_i = sb("iota_i", [P, BANK], I32)
        loaded, small, turned, made, chain = sem("loaded"), sem("small"), sem("turned"), sem("made"), sem("chain")
        edges_in, x_in, ev = sem("edges_in"), sem("x_in"), sem("ev")
        G, T = s.NG, s.TG
        block = ctx.enter_context(nc.Block())

        @block.sync
        def _(sp):
            for n in ("src", "dst"):
                sp.dma_start(ed[n][0:G, :], t[n].rearrange("(g e) -> g e", g=G)).then_inc(edges_in, 16)
            sp.dma_start(k["x"][0:s.NP, :].rearrange("p (b d) -> p b d", d=D),
                         t["x"].rearrange("(b p) d -> p b d", p=s.NP)).then_inc(x_in, 16)
            for n in raw:
                sp.dma_start(raw[n][:, :], t["L0_gnn_" + n]).then_inc(loaded, 16)
            for n in ("b1", "b2", "b3"):
                sp.dma_start(k[n][:, :], t["L0_gnn_" + n].rearrange("(a d) -> a d", a=1)).then_inc(small, 16)
            sp.dma_start(epst[:, :], t["L1_gnn_eps"].rearrange("(a d) -> a d", a=1)).then_inc(small, 16)
            sp.wait_ge(small, 16 * 4)
            sp.wait_ge(x_in, 16)

        @block.gpsimd
        def _(pool):
            nc.gpsimd.iota(iota_i[:, :], pattern=[[1, BANK]], base=0, channel_multiplier=0).then_inc(made, 1)
            nc.gpsimd.memset(k["ident"][:, :], 0.0).then_inc(chain, 1)
            pool.wait_ge(chain, 1)
            nc.gpsimd.affine_select(out=k["ident"][:, :], in_=k["ident"][:, :], compare_op=ALU.not_equal,
                                    fill=1.0, base=0, pattern=[[-1, P]], channel_multiplier=1).then_inc(made, 1)
            nc.gpsimd.memset(k["ones"][:, :], 1.0).then_inc(made, 1)
            nc.gpsimd.memset(k["zeros"][:, :], 0.0).then_inc(made, 1)

        @block.vector
        def _(dve):
            n = [0]

            def step(ins):
                n[0] += 1
                ins.then_inc(ev, 1)
                dve.wait_ge(ev, n[0])
            step(dve.memset(k["src_idx"][:, :], 0))
            dve.wait_ge(edges_in, 32)
            step(dve.tensor_copy(srcf[0:G, :], ed["src"][0:G, :]))
            step(dve.tensor_copy(dstf[0:G, :], ed["dst"][0:G, :]))
            step(dve.tensor_reduce(col[0:G, 0:1], dstf[0:G, :], AX.X, ALU.min))
            step(dve.tensor_reduce(col[0:G, 1:2], dstf[0:G, :], AX.X, ALU.max))
            step(dve.tensor_scalar(relf[0:G, :], dstf[0:G, :], col[0:G, 0:1], None, ALU.subtract))
            step(dve.tensor_scalar(col[0:G, 3:4], col[0:G, 1:2], col[0:G, 0:1], float(s.W), ALU.subtract, ALU.is_ge))
            dve.wait_ge(turned, 1)
            for i, (dst, m) in enumerate((("src_idx", 0), ("dst_abs", 1), ("dst_rel", 2))):
                step(dve.tensor_copy(k[dst][0:s.EP, 0:s.NT].rearrange("p (g j) -> p j g", j=T),
                                     k["ps"][0:s.EP, m * BANK:m * BANK + T * G].rearrange("p (j g) -> p j g", j=T)))
            step(dve.tensor_copy(k["starts"][0:1, :], k["ps"][0:1, 3 * BANK:3 * BANK + G]))
            step(dve.tensor_reduce(viol[0:1, :], k["ps"][0:1, 3 * BANK + G:3 * BANK + 2 * G], AX.X, ALU.max))
            step(dve.tensor_copy(k["spill"][0:1, :], viol[0:1, :]))
            dve.wait_ge(made, 1)
            step(dve.tensor_copy(k["iota"][:, :], iota_i[:, :]))
            step(dve.tensor_copy(k["iota16"][:, :], iota_i[:, :]))
            dve.wait_ge(turned, 2)
            for i, w in enumerate(raw):
                step(dve.tensor_copy(k[w][:, :], k["ps"][:, 4 * BANK + i * D:4 * BANK + (i + 1) * D]))
            step(dve.tensor_scalar(k["eps1"][:, :], k["ps"][:, 6 * BANK:6 * BANK + 1], 1.0, None, ALU.add))

        @block.tensor
        def _(pe):
            pe.wait_ge(made, 4)
            pe.wait_ge(ev, 7)
            for m, a in enumerate((srcf, dstf, relf)):
                for j in range(T):
                    pe.transpose(k["ps"][0:s.EP, m * BANK + j * G:m * BANK + (j + 1) * G],
                                 a[0:G, j:s.EP * T:T], k["ident"][0:G, 0:G])
            pe.transpose(k["ps"][0:1, 3 * BANK:3 * BANK + G], col[0:G, 0:1], k["ident"][0:G, 0:G])
            pe.transpose(k["ps"][0:1, 3 * BANK + G:3 * BANK + 2 * G], col[0:G, 3:4],
                         k["ident"][0:G, 0:G]).then_inc(turned, 1)
            pe.wait_ge(loaded, 16 * 6)
            for i, w in enumerate(raw):
                pe.transpose(k["ps"][:, 4 * BANK + i * D:4 * BANK + (i + 1) * D], raw[w][:, :], k["ident"][:, :])
            pe.wait_ge(small, 16 * 4)
            pe.matmul(k["ps"][:, 6 * BANK:6 * BANK + 1], k["ones"][0:1, :], epst[0:1, 0:1],
                      start=True, stop=True).then_inc(turned, 1)


def layer_norm(nc, s, k, name):
    with ExitStack() as ctx:
        st = ctx.enter_context(nc.sbuf_tensor(name + "_st", [P, 4, s.NB], F32))
        sq = ctx.enter_context(nc.sbuf_tensor(name + "_sq", [P, s.NB, D], F32))
        sem = semaphores(nc, ctx, name)
        dn, rt = sem("_dn"), sem("_rt")
        block = ctx.enter_context(nc.Block())
        x = k["x"][0:s.NP, :].rearrange("p (b d) -> p b d", d=D)
        h = k["hn"][0:s.NP, :].rearrange("p (b d) -> p b d", d=D)
        q = sq[0:s.NP, :, :]

        def bc(i):
            return st[0:s.NP, i, :].rearrange("p (b a) -> p b a", a=1).to_broadcast([s.NP, s.NB, D])

        @block.vector
        def _(dve):
            n = [0]

            def step(ins):
                n[0] += 1
                ins.then_inc(dn, 1)
                dve.wait_ge(dn, n[0])
            step(dve.tensor_reduce(st[0:s.NP, 0, :], x, AX.X, ALU.add))
            step(dve.tensor_scalar(st[0:s.NP, 1, :], st[0:s.NP, 0, :], 1.0 / D, None, ALU.mult))
            step(dve.tensor_tensor(h, x, bc(1), ALU.subtract))
            step(dve.tensor_tensor(q, h, h, ALU.mult))
            step(dve.tensor_reduce(st[0:s.NP, 2, :], q, AX.X, ALU.add))
            step(dve.tensor_scalar(st[0:s.NP, 3, :], st[0:s.NP, 2, :], 1.0 / D, EPS_LN, ALU.mult, ALU.add))
            dve.wait_ge(rt, 1)
            step(dve.reciprocal(st[0:s.NP, 1, :], st[0:s.NP, 0, :]))
            step(dve.tensor_tensor(q, h, bc(1), ALU.mult))
            step(dve.tensor_scalar(h, q, 0.0, None, ALU.max))

        @block.scalar
        def _(act):
            act.wait_ge(dn, 6)
            act.activation(st[0:s.NP, 0, :], st[0:s.NP, 3, :], ACT.Sqrt).then_inc(rt, 1)


def turn_rows(nc, s, k, table, weight, name):
    with ExitStack() as ctx:
        sem = semaphores(nc, ctx, name)
        turned, kept, mixed, out_ready, stored = sem("t"), sem("k"), sem("m"), sem("o"), sem("s")
        g = ctx.enter_context(nc.sbuf_tensor(name + "_g", [P, s.NB, D], F32))
        block = ctx.enter_context(nc.Block())
        per = BANK // D
        nch = -(-s.NB // per)

        @block.tensor
        def _(pe):
            for c in range(nch):
                for b in range(c * per, min(s.NB, (c + 1) * per)):
                    ins = pe.transpose(k["ps"][:, (c % 7) * BANK + (b % per) * D:(c % 7) * BANK + (b % per) * D + s.NP],
                                       k["hn"][0:s.NP, b * D:(b + 1) * D], k["ident"][0:s.NP, 0:s.NP])
                ins.then_inc(turned, 1)
            if weight:
                for b in range(s.NB):
                    if b % per == 0:
                        pe.wait_ge(kept, nch)
                        if b:
                            pe.wait_ge(out_ready, b // per)
                    o = k["ps"][0:s.NP, (7 * BANK + (b % per) * D):(7 * BANK + (b % per + 1) * D)]
                    pe.matmul(o, k["hT"][:, b * s.NP:(b + 1) * s.NP], k[weight][:, :], start=True, stop=False)
                    ins = pe.matmul(o, k["ones"][0:1, 0:s.NP], k["be1"][0:1, :], start=False, stop=True)
                    if b % per == per - 1 or b == s.NB - 1:
                        ins.then_inc(mixed, 1)

        @block.vector
        def _(dve):
            hT = k["hT"][:, :].rearrange("f (b p) -> f b p", b=s.NB)
            for c in range(nch):
                nb = min(per, s.NB - c * per)
                dve.wait_ge(turned, c + 1)
                dve.tensor_copy(hT[:, c * per:c * per + nb, :],
                                k["ps"][:, (c % 7) * BANK:(c % 7) * BANK + nb * D].rearrange(
                                    "f (b q) -> f b q", q=D)[:, :, 0:s.NP]).then_inc(kept, 1)
            if weight:
                for c in range(nch):
                    nb = min(per, s.NB - c * per)
                    dve.wait_ge(mixed, c + 1)
                    dve.tensor_copy(g[0:s.NP, c * per:c * per + nb, :],
                                    k["ps"][0:s.NP, 7 * BANK:7 * BANK + nb * D].rearrange("p (b d) -> p b d", d=D)).then_inc(out_ready, 1)

        @block.sync
        def _(sp):
            src = k["hn"][0:s.NP, :].rearrange("p (b d) -> p b d", d=D)
            if weight:
                src = g[0:s.NP, :, :]
                sp.wait_ge(out_ready, nch)
            sp.dma_start(table.rearrange("(b p) d -> p b d", p=s.NP), src).then_inc(stored, 16)
            sp.wait_ge(stored, 16)


def zero_sums(nc, s, k, n):
    with ExitStack() as ctx:
        block = ctx.enter_context(nc.Block())

        @block.tensor
        def _(pe):
            for c in range(n):
                pe.matmul(k["ps"][:, c * BANK:(c + 1) * BANK], k["zeros"][:, 0:P], k["zeros"][:, :],
                          start=True, stop=False, skip_group_check=True)


def take_sums(nc, s, k, first, n):
    with ExitStack() as ctx:
        block = ctx.enter_context(nc.Block())

        @block.vector
        def _(dve):
            for c in range(first, first + n):
                dve.tensor_copy(k["aT"][:, c * BANK:c * BANK + chunk(s, c)],
                                k["ps"][:, (c - first) * BANK:(c - first) * BANK + chunk(s, c)])


def tile_loop(eng, s, step):
    n = s.NT // RING
    with eng.Fori(0, n) as i:
        for j in range(RING):
            step(i, j)
    for j in range(s.NT - n * RING):
        step(n, j)


def ahead(s, i, j, d):
    if isinstance(i, int) and i * RING + j + d >= s.NT:
        return None
    return (i, j + d) if j + d < RING else (i + 1, j + d - RING)


def edge_pass(nc, s, t, k, table, kind, chunks, name):
    windowed = chunks is None
    first, n_ch = chunks or (0, 0)
    W = s.W if windowed else sum(chunk(s, first + c) for c in range(n_ch))
    gine, sage = kind == "gine", kind == "sage"
    R, Z = SB_RING, PS_RING
    OR = R if windowed else 1
    LEAD = RING - OR
    TC = s.TG + 1
    dst = k["dst_rel"] if windowed else k["dst_abs"]
    with ExitStack() as ctx:
        def sb(n, shape, dt=F32):
            return ctx.enter_context(nc.sbuf_tensor(name + n, shape, dt))

        sem = semaphores(nc, ctx, name)
        onehot = sb("_oh", [P, OR, W])
        oh_ready, agg_done, added = sem("_oh_ready"), sem("_agg_done"), sem("_added")
        if kind != "count":
            rows = sb("_rows", [P, RING, D])
            slot_idx = sb("_idx", [P, RING], I32)
            slot_ready, started = sem("_slot_ready"), sem("_started")
            gathered = [sem(f"_gathered{j}") for j in range(RING)]
        if gine:
            ea = sb("_ea", [P, 2, s.TG * D])
            eaT = sb("_eaT", [P, R, P])
            pre = sb("_pre", [P, R, D])
            msg = sb("_msg", [P, R, D])
            ea_in = [sem(f"_ea_in{h}") for h in range(2)]
            eaT_ps, eaT_ready = sem("_eaT_ps"), sem("_eaT_ready")
            z_ready, pre_ready, msg_ready = sem("_z_ready"), sem("_pre_ready"), sem("_msg_ready")

        def z_ps(j):
            return k["ps"][0:s.EP, (6 + j % Z) * BANK:(6 + j % Z) * BANK + D]

        def t_ps(j):
            return k["ps"][:, (4 + j % Z) * BANK:(4 + j % Z) * BANK + s.EP]
        block = ctx.enter_context(nc.Block())

        if kind != "count":
            @block.gpsimd
            def _(pool):
                def step(i, j):
                    pool.wait_ge(slot_ready, i * RING + j + 1)
                    pool.sem_inc(started, 1)
                    pool.indirect_dma_start(
                        out=rows[0:s.EP, j, :], out_offset=None, in_=table,
                        in_offset=bass.IndirectOffsetOnAxis(ap=slot_idx[0:s.EP, j:j + 1], axis=0),
                    ).then_inc(gathered[j], 16)
                tile_loop(pool, s, step)

        if gine:
            @block.sync
            def _(sp):
                def load(i, h):
                    g = i * 2 + h
                    sp.wait_ge(eaT_ps, g * s.TG + 1)
                    sp.dma_start(ea[0:s.EP, h, :],
                                 t["edge_attr_128"][bass.ds(g * (s.EP * s.TG), s.EP * s.TG), :].rearrange(
                                     "(p j) d -> p (j d)", j=s.TG)).then_inc(ea_in[h], 16)
                with sp.Fori(0, s.NG // 2) as i:
                    for h in range(2):
                        load(i, h)
                load(s.NG // 2, 0)

        @block.vector
        def _(dve):
            dve.sem_inc(oh_ready, OR)
            if windowed:
                dve.memset(k["aT"][:, :], 0.0).then_inc(added, 2)

            def add_window(i, h):
                g = 2 * i + h
                base = dve.value_load(k["starts"][0:1, bass.ds(g, 1)], min_val=0, max_val=s.N - 1)
                window = k["aT"][:, bass.ds(base, s.W)]
                dve.wait_ge(agg_done, (g + 1) * s.TG + OR)
                dve.wait_ge(added, g + 2)
                dve.tensor_tensor(window, window, k["ps"][:, h * BANK:h * BANK + s.W], ALU.add).then_inc(added, 1)

            if gine:
                dve.sem_inc(pre_ready, R)
            if kind != "count":
                dve.tensor_copy(slot_idx[0:s.EP, 0:LEAD], k["src_idx"][0:s.EP, 0:LEAD]).then_inc(slot_ready, LEAD)

            def step(i, j):
                tt = i * RING + j
                dve.wait_ge(agg_done, tt + 1)
                if windowed:
                    dve.tensor_scalar(onehot[0:s.EP, j % OR, :], k["iota"][0:s.EP, 0:W], dst[0:s.EP, bass.ds(tt, 1)],
                                      None, ALU.is_equal).then_inc(oh_ready, 1)
                else:
                    for c in range(n_ch):
                        w = chunk(s, first + c)
                        ins = dve.tensor_scalar(onehot[0:s.EP, 0, c * BANK:c * BANK + w], k["iota"][0:s.EP, 0:w],
                                                float((first + c) * BANK), dst[0:s.EP, bass.ds(tt, 1)],
                                                ALU.add, ALU.is_equal)
                    ins.then_inc(oh_ready, 1)
                if kind != "count":
                    q = (j + LEAD) % RING
                    dve.tensor_copy(slot_idx[0:s.EP, q:q + 1],
                                    k["src_idx"][0:s.EP, bass.ds(tt + LEAD, 1)]).then_inc(slot_ready, 1)
                if gine:
                    dve.wait_ge(z_ready, tt + 1 + Z)
                    dve.wait_ge(gathered[j], (i + 1) * 16)
                    dve.wait_ge(msg_ready, tt + 1)
                    dve.tensor_tensor(pre[0:s.EP, j % R, :], z_ps(j), rows[0:s.EP, j, :],
                                      ALU.add).then_inc(pre_ready, 1)
                if windowed and j == s.TG + 3:
                    add_window(i, 0)
            if not windowed:
                tile_loop(dve, s, step)
            else:
                n = s.NT // RING
                with dve.Fori(0, n) as i:
                    for j in range(RING):
                        step(i, j)
                    add_window(i, 1)
                for j in range(s.NT - n * RING):
                    step(n, j)
                add_window(n, 0)

        if gine:
            @block.scalar
            def _(act):
                act.sem_inc(eaT_ready, R)
                act.sem_inc(msg_ready, R)

                def turn_out(i, j):
                    tt = i * RING + j
                    act.wait_ge(eaT_ps, tt + 1 + TC)
                    act.copy(eaT[:, j % R, 0:s.EP], t_ps(j)).then_inc(eaT_ready, 1)

                def step(i, j):
                    tt = i * RING + j
                    act.wait_ge(pre_ready, tt + 1 + R)
                    act.wait_ge(agg_done, tt + 1)
                    act.activation(msg[0:s.EP, j % R, :], pre[0:s.EP, j % R, :], ACT.Gelu).then_inc(msg_ready, 1)
                    a = ahead(s, i, j, 3)
                    if a:
                        turn_out(*a)
                for j in range(3):
                    turn_out(0, j)
                tile_loop(act, s, step)

        @block.tensor
        def _(pe):
            pe.sem_inc(agg_done, OR)
            if gine:
                pe.sem_inc(eaT_ps, TC)
                pe.sem_inc(z_ready, Z)

            def turn(i, j):
                tt = i * RING + j
                if j % s.TG == 0:
                    pe.wait_ge(ea_in[j // s.TG], (i + 1) * 16)
                pe.wait_ge(eaT_ready, tt + 1 + R - Z)
                pe.transpose(t_ps(j), ea[0:s.EP, j // s.TG, (j % s.TG) * D:(j % s.TG + 1) * D],
                             k["ident"][0:s.EP, 0:s.EP]).then_inc(eaT_ps, 1)

            def mix(i, j):
                tt = i * RING + j
                pe.wait_ge(eaT_ready, tt + 1 + R)
                pe.wait_ge(pre_ready, tt + 1 + R - Z)
                pe.matmul(z_ps(j), eaT[:, j % R, 0:s.EP], k["We1"][:, :], start=True, stop=True).then_inc(z_ready, 1)

            def step(i, j):
                tt = i * RING + j
                if gine:
                    a = ahead(s, i, j, 3)
                    if a:
                        turn(*a)
                    a = ahead(s, i, j, 2)
                    if a:
                        mix(*a)
                if windowed and j % s.TG == 0:
                    pe.wait_ge(added, 2 * i + j // s.TG + 1)
                pe.wait_ge(oh_ready, tt + 1 + OR)
                if gine:
                    pe.wait_ge(msg_ready, tt + 1 + R)
                    message = msg[0:s.EP, j % R, :]
                elif sage:
                    pe.wait_ge(gathered[j], (i + 1) * 16)
                    message = rows[0:s.EP, j, :]
                else:
                    message = k["ones"][0:s.EP, :]
                if windowed:
                    h = j // s.TG
                    ins = pe.matmul(k["ps"][:, h * BANK:h * BANK + s.W], message, onehot[0:s.EP, j % OR, :],
                                    start=j % s.TG == 0, stop=j % s.TG == s.TG - 1)
                else:
                    for c in range(n_ch):
                        w = chunk(s, first + c)
                        ins = pe.matmul(k["ps"][:, c * BANK:c * BANK + w], message,
                                        onehot[0:s.EP, j % OR, c * BANK:c * BANK + w],
                                        start=False, stop=False, skip_group_check=True)
                ins.then_inc(agg_done, 1)
            if gine:
                for j in range(3):
                    turn(0, j)
                for j in range(2):
                    mix(0, j)
            tile_loop(pe, s, step)


def take_counts(nc, s, k):
    with ExitStack() as ctx:
        done = semaphores(nc, ctx)("counts_done")
        block = ctx.enter_context(nc.Block())

        @block.vector
        def _(dve):
            dve.tensor_copy(k["cnt1"][0:1, :], k["aT"][0:1, 0:s.N]).then_inc(done, 1)
            dve.wait_ge(done, 1)
            dve.tensor_scalar(k["aT"][:, 0:s.N], k["aT"][:, 0:s.N], 1.0, None, ALU.max).then_inc(done, 1)
            dve.wait_ge(done, 2)
            dve.reciprocal(k["rcntT"][:, :], k["aT"][:, 0:s.N]).then_inc(done, 1)
            dve.wait_ge(done, 3)


def sage_nodes(nc, s, k, table, layer):
    last = layer == 3
    with ExitStack() as ctx:
        sem = semaphores(nc, ctx, f"nodes{layer}_")
        mean_ready, mixed, new_ready, turned, rows_ready, stored = (
            sem("mean_ready"), sem("mixed"), sem("new_ready"), sem("turned"), sem("rows_ready"), sem("stored"))
        block = ctx.enter_context(nc.Block())
        per = BANK // D
        nq = -(-s.NB // per)

        def cols(name, c):
            return k[name][:, c * BANK:c * BANK + chunk(s, c)]

        @block.vector
        def _(dve):
            for c in range(s.CH):
                dve.tensor_tensor(cols("aT", c), cols("aT", c), cols("rcntT", c), ALU.mult).then_inc(mean_ready, 1)
            for q in range(nq):
                nb = min(per, s.NB - q * per)
                dve.wait_ge(turned, q + 1)
                src = k["ps"][0:s.NP, q * BANK:q * BANK + nb * D]
                dve.tensor_copy(k["hn"][0:s.NP, q * BANK:q * BANK + nb * D], src).then_inc(rows_ready, 1)

        @block.tensor
        def _(pe):
            for c in range(s.CH):
                pe.wait_ge(mean_ready, c + 1)
                pe.matmul(cols("ps", c), k[f"W{layer}l"][:, :], cols("aT", c), start=True, stop=False)
                pe.matmul(cols("ps", c), k[f"W{layer}r"][:, :], cols("hT", c), start=False, stop=True).then_inc(mixed, 1)
            pe.wait_ge(new_ready, s.CH)
            for q in range(nq):
                for b in range(q * per, min(s.NB, (q + 1) * per)):
                    ins = pe.transpose(k["ps"][0:s.NP, b * D:(b + 1) * D], k["hT"][:, b * s.NP:(b + 1) * s.NP], k["ident"][:, :])
                ins.then_inc(turned, 1)

        @block.scalar
        def _(act):
            for c in range(s.CH):
                act.wait_ge(mixed, c + 1)
                act.activation(cols("hT", c), cols("ps", c), ACT.Identity if last else ACT.Relu,
                               bias=k[f"b{layer}c"][:, 0:1]).then_inc(new_ready, 1)

        if not last:
            @block.sync
            def _(sp):
                sp.wait_ge(rows_ready, nq)
                sp.dma_start(table.rearrange("(b p) d -> p b d", p=s.NP), k["hn"][0:s.NP, :].rearrange("p (b d) -> p b d", d=D)).then_inc(stored, 16)
                sp.wait_ge(stored, 16)


def gine_nodes(nc, s, k, out):
    with ExitStack() as ctx:
        sem = semaphores(nc, ctx, "gine_nodes_")
        msg_mixed, u_ready, v_mixed, v_ready, y_mixed, y_ready, stored = (
            sem("msg_mixed"), sem("u_ready"), sem("v_mixed"), sem("v_ready"), sem("y_mixed"),
            sem("y_ready"), sem("stored"))
        block = ctx.enter_context(nc.Block())
        per = BANK // D
        nq = -(-s.NB // per)

        def cols(name, c):
            return k[name][:, c * BANK:c * BANK + chunk(s, c)]

        @block.vector
        def _(dve):
            for c in range(s.CH):
                dve.wait_ge(msg_mixed, c + 1)
                dve.scalar_tensor_tensor(out=cols("rcntT", c), in0=cols("hT", c), scalar=k["eps1"][:, 0:1],
                                         in1=cols("ps", c), op0=ALU.mult, op1=ALU.add).then_inc(u_ready, 1)
            for q in range(nq):
                w = min(per, s.NB - q * per) * D
                dve.wait_ge(y_mixed, q + 1)
                dve.tensor_tensor(k["x"][0:s.NP, q * BANK:q * BANK + w], k["x"][0:s.NP, q * BANK:q * BANK + w],
                                  k["ps"][0:s.NP, q * BANK:q * BANK + w], ALU.add).then_inc(y_ready, 1)

        @block.tensor
        def _(pe):
            for c in range(s.CH):
                pe.matmul(cols("ps", c), k["We2"][:, :], cols("aT", c), start=True, stop=False)
                pe.matmul(cols("ps", c), k["be2"][0:1, :], k["cnt1"][0:1, c * BANK:c * BANK + chunk(s, c)],
                          start=False, stop=True).then_inc(msg_mixed, 1)
            for c in range(s.CH):
                pe.wait_ge(u_ready, c + 1)
                pe.matmul(cols("ps", c), k["Wu1"][:, :], cols("rcntT", c), start=True, stop=True).then_inc(v_mixed, 1)
            pe.wait_ge(v_ready, s.CH)
            for q in range(nq):
                for b in range(q * per, min(s.NB, (q + 1) * per)):
                    o = k["ps"][0:s.NP, b * D:(b + 1) * D]
                    pe.matmul(o, k["hT"][:, b * s.NP:(b + 1) * s.NP], k["Wu2"][:, :], start=True, stop=False)
                    ins = pe.matmul(o, k["ones"][0:1, 0:s.NP], k["bu2"][0:1, :], start=False, stop=True)
                ins.then_inc(y_mixed, 1)

        @block.scalar
        def _(act):
            for c in range(s.CH):
                act.wait_ge(v_mixed, c + 1)
                act.activation(cols("hT", c), cols("ps", c), ACT.Gelu, bias=k["bu1"][:, 0:1]).then_inc(v_ready, 1)

        @block.sync
        def _(sp):
            sp.wait_ge(y_ready, nq)
            sp.dma_start(out.rearrange("(b p) d -> p b d", p=s.NP),
                         k["x"][0:s.NP, :].rearrange("p (b d) -> p b d", d=D)).then_inc(stored, 16)
            sp.wait_ge(stored, 16)


def save_lists(nc, s, k, lists):
    with ExitStack() as ctx:
        stored = semaphores(nc, ctx)("lists_stored")
        block = ctx.enter_context(nc.Block())

        @block.sync
        def _(sp):
            sp.dma_start(lists["src_idx"][:, :], k["src_idx"][:, :]).then_inc(stored, 16)
            for n in ("dst_abs", "dst_rel"):
                sp.dma_start(lists[n][0:s.EP, 0:s.NT], k[n][0:s.EP, :]).then_inc(stored, 16)
            sp.wait_ge(stored, 48)


def load_second(nc, s, t, k, lists):
    with ExitStack() as ctx:
        sem = semaphores(nc, ctx)
        loaded, made = sem("second_loaded"), sem("second_made")
        iota_i = ctx.enter_context(nc.sbuf_tensor("iota_i2", [P, BANK], I32))
        block = ctx.enter_context(nc.Block())

        @block.sync
        def _(sp):
            sp.dma_start(k["src_idx"][:, :], lists["src_idx"][:, :]).then_inc(loaded, 16)
            for n in ("dst_abs", "dst_rel"):
                sp.dma_start(k[n][0:s.EP, :], lists[n][0:s.EP, 0:s.NT]).then_inc(loaded, 16)
            sp.dma_start(k["x"][0:s.NP, :].rearrange("p (b d) -> p b d", d=D),
                         t["x"].rearrange("(b p) d -> p b d", p=s.NP)).then_inc(loaded, 16)
            for n in ("We1", "We2", "Wu1", "Wu2"):
                sp.dma_start(k[n][:, :], t["L1_gnn_" + n]).then_inc(loaded, 16)
            for n in ("b1", "b2", "b3"):
                sp.dma_start(k[n + "c"][:, :], t["L0_gnn_" + n].rearrange("(d a) -> d a", a=1)).then_inc(loaded, 16)
            sp.dma_start(k["bu1"][:, :], t["L1_gnn_bu1"].rearrange("(d a) -> d a", a=1)).then_inc(loaded, 16)
            for n in ("be1", "be2", "bu2"):
                sp.dma_start(k[n][:, :], t["L1_gnn_" + n].rearrange("(a d) -> a d", a=1)).then_inc(loaded, 16)
            sp.wait_ge(loaded, 16 * 15)

        @block.gpsimd
        def _(pool):
            nc.gpsimd.iota(iota_i[:, :], pattern=[[1, BANK]], base=0, channel_multiplier=0).then_inc(made, 1)
            nc.gpsimd.memset(k["zeros"][:, :], 0.0)
            pool.wait_ge(made, 1)
            nc.gpsimd.tensor_copy(k["iota"][:, :], iota_i[:, :])


def residual(nc, s, k):
    with ExitStack() as ctx:
        block = ctx.enter_context(nc.Block())

        @block.vector
        def _(dve):
            dve.tensor_tensor(k["x"][0:s.NP, :], k["x"][0:s.NP, :], k["hn"][0:s.NP, :], ALU.add)


def dense_keys(nc, s, t, k):
    main, half, tail = s.DG // 2, s.EP * s.DT, s.EP
    with ExitStack() as ctx:
        def sb(name, shape, dt=F32):
            return ctx.enter_context(nc.sbuf_tensor("dk_" + name, shape, dt))
        sem = semaphores(nc, ctx, "dk_")
        raw = {(n, part): sb(f"{n}_{part}", [main if part == "m" else 1, 2 * half if part == "m" else tail], I32)
               for n in ("src", "dst") for part in "mt"}
        w = {(n, part): sb(f"{n}f_{part}", [main if part == "m" else 1, 2 * half if part == "m" else tail],
                           I32 if n == "qi" else F32)
             for n in ("src", "dst", "qi", "q", "r", "fix", "key") for part in "mt"}
        ends = {"m": sb("ends_m", [main, 4]), "t": sb("ends_t", [1, 4])}
        row = sb("row", [1, 2, s.DG + 1])
        viol = sb("viol", [1, 6, s.DG + 1])
        top = sb("top", [1, 2])
        steps = w["fix", "m"][0:1, 0:s.DG]
        loaded, turned, ev = sem("loaded"), sem("turned"), sem("ev")
        block = ctx.enter_context(nc.Block())
        ps = k["ps"]
        n_main = [0]

        @block.sync
        def _(sp):
            for n in ("src", "dst"):
                sp.dma_start(raw[n, "m"][:, :], t[n][0:main * 2 * half].rearrange("(g e) -> g e", g=main)
                             ).then_inc(loaded, 16)
                sp.dma_start(raw[n, "t"][:, :], t[n][main * 2 * half:s.E].rearrange("(a e) -> a e", a=1)
                             ).then_inc(loaded, 16)

        @block.vector
        def _(dve):
            def step(ins):
                n_main[0] += 1
                ins.then_inc(ev, 1)
                dve.wait_ge(ev, n_main[0])
            dve.wait_ge(loaded, 64)
            for part, groups in (("m", 2), ("t", 1)):
                src, dst, qi, q, r, fix, key = (w[n, part][:, :] for n in ("src", "dst", "qi", "q", "r", "fix", "key"))
                step(dve.tensor_copy(src, raw["src", part][:, :]))
                step(dve.tensor_copy(dst, raw["dst", part][:, :]))
                step(dve.tensor_scalar(r, src, -float(s.NP // 2), 1.0 / s.NP, ALU.add, ALU.mult))
                step(dve.tensor_copy(qi, r))
                step(dve.tensor_copy(q, qi))
                step(dve.scalar_tensor_tensor(out=r, in0=q, scalar=-float(s.NP), in1=src, op0=ALU.mult, op1=ALU.add))
                step(dve.tensor_scalar(fix, r, float(s.NP), None, ALU.is_ge))
                step(dve.tensor_tensor(q, q, fix, ALU.add))
                step(dve.scalar_tensor_tensor(out=r, in0=fix, scalar=-float(s.NP), in1=r, op0=ALU.mult, op1=ALU.add))
                step(dve.tensor_scalar(fix, r, 0.0, None, ALU.is_lt))
                step(dve.tensor_tensor(q, q, fix, ALU.subtract))
                step(dve.scalar_tensor_tensor(out=r, in0=fix, scalar=float(s.NP), in1=r, op0=ALU.mult, op1=ALU.add))
                e = ends[part]
                for h in range(groups):
                    n = half if part == "m" else tail
                    d = w["dst", part][:, h * n:(h + 1) * n]
                    step(dve.tensor_reduce(e[:, h:h + 1], d, AX.X, ALU.min))
                    step(dve.tensor_reduce(e[:, 2 + h:3 + h], d, AX.X, ALU.max))
                    kk = w["key", part][:, h * n:(h + 1) * n]
                    step(dve.tensor_scalar(kk, d, e[:, h:h + 1], float(s.NB), ALU.subtract, ALU.mult))
                    step(dve.tensor_tensor(kk, kk, w["q", part][:, h * n:(h + 1) * n], ALU.add))
            n_main.append(n_main[0])
            dve.wait_ge(turned, 1)
            for i, a in enumerate(("key", "low")):
                step(dve.tensor_copy(k[a][0:s.EP, 0:4 * main].rearrange("p (i q) -> p q i", q=4),
                                     ps[0:s.EP, i * BANK:i * BANK + 4 * main].rearrange("p (q i) -> p q i", q=4)))
                step(dve.tensor_copy(k[a][0:s.EP, 4 * main:4 * main + 1], ps[0:s.EP, 2 * BANK + i:2 * BANK + i + 1]))
            for i in range(2):
                step(dve.tensor_copy(row[:, i, 0:s.DG].rearrange("a (i h) -> a h i", h=2),
                                     ps[0:1, 3 * BANK + 2 * i * main:3 * BANK + 2 * (i + 1) * main].rearrange(
                                         "a (h i) -> a h i", h=2)))
                step(dve.tensor_copy(row[:, i, s.DG:s.DG + 1], ends["t"][:, 2 * i:2 * i + 1]))
            G = s.DG
            step(dve.memset(viol[:, :, :], 0.0))
            lo, hi = row[:, 0, :], row[:, 1, :]
            step(dve.tensor_tensor(viol[:, 0, :], hi, lo, ALU.subtract))
            step(dve.tensor_scalar(viol[:, 0, :], viol[:, 0, :], float(s.DW), None, ALU.is_ge))
            step(dve.tensor_tensor(viol[:, 1, 0:G], lo[:, 1:G + 1], hi[:, 0:G], ALU.is_lt))
            step(dve.tensor_tensor(viol[:, 4, 0:G], lo[:, 1:G + 1], lo[:, 0:G], ALU.subtract))
            step(dve.tensor_scalar(steps[:, 0:G], viol[:, 4, 0:G], float(s.NB), None, ALU.mult))
            n_main.append(n_main[0])
            step(dve.tensor_copy(k["dstarts"][:, :], lo))
            step(dve.tensor_scalar(viol[:, 2, 0:G], viol[:, 4, 0:G], float(s.DW), None, ALU.is_ge))
            step(dve.tensor_tensor(viol[:, 5, 0:G - 1], lo[:, 2:G + 1], hi[:, 0:G - 1], ALU.is_le))
            step(dve.tensor_scalar(viol[:, 3, 0:1], lo[:, 0:1], 0.0, None, ALU.is_gt))
            step(dve.tensor_scalar(viol[:, 3, 1:2], lo[:, G:G + 1], float(s.N - s.DW), None, ALU.is_lt))
            step(dve.tensor_reduce(top[:, 0:1], viol[:, 0:4, :].rearrange("a b c -> a (b c)"), AX.X, ALU.max))
            step(dve.tensor_reduce(top[:, 1:2], viol[:, 5, :], AX.X, ALU.max))
            step(dve.tensor_tensor(top[:, 0:1], top[:, 0:1], top[:, 1:2], ALU.max))
            step(dve.tensor_copy(top[:, 1:2], k["spill"][:, :]))
            step(dve.tensor_tensor(top[:, 0:1], top[:, 0:1], top[:, 1:2], ALU.max))
            step(dve.tensor_copy(k["spill"][:, :], top[:, 0:1]))
            dve.wait_ge(turned, 2)
            wide = [s.EP, G, s.DT]
            step(dve.tensor_tensor(
                k["next_key"][0:s.EP, 0:G * s.DT].rearrange("p (g j) -> p g j", j=s.DT),
                k["key"][0:s.EP, 0:G * s.DT].rearrange("p (g j) -> p g j", j=s.DT),
                ps[0:s.EP, 4 * BANK:4 * BANK + G].rearrange("p (g a) -> p g a", a=1).to_broadcast(wide), ALU.subtract))

        @block.tensor
        def _(pe):
            pe.wait_ge(ev, n_main[1])
            for i, a in enumerate(("key", "r")):
                for h in range(2):
                    for j in range(s.DT):
                        q = h * s.DT + j
                        pe.transpose(ps[0:s.EP, i * BANK + q * main:i * BANK + (q + 1) * main],
                                     w[a, "m"][:, h * half + j:(h + 1) * half:s.DT], k["ident"][0:main, 0:main])
                pe.transpose(ps[0:s.EP, 2 * BANK + i:2 * BANK + i + 1], w[a, "t"][:, :], k["ident"][0:1, 0:1])
            for q in range(4):
                ins = pe.transpose(ps[0:1, 3 * BANK + q * main:3 * BANK + (q + 1) * main], ends["m"][:, q:q + 1],
                                   k["ident"][0:main, 0:main])
            ins.then_inc(turned, 1)
            pe.wait_ge(ev, n_main[2])
            pe.matmul(ps[0:s.EP, 4 * BANK:4 * BANK + s.DG], k["ones"][0:1, 0:s.EP], steps[:, :],
                      start=True, stop=True).then_inc(turned, 1)


def build_adjacency(nc, s, k):
    U = 4
    CREDIT = U - 1
    EVEN = s.NP + s.NP % 2
    cols = s.NB * s.DW
    G = s.DG
    with ExitStack() as ctx:
        sem = semaphores(nc, ctx, "adj_")
        keys = ctx.enter_context(nc.sbuf_tensor("key_onehot", [P, U, s.DT, cols], F16))
        lows = ctx.enter_context(nc.sbuf_tensor("low_onehot", [P, U, s.DT, P], F16))
        nexts = ctx.enter_context(nc.sbuf_tensor("next_onehot", [P, U, s.DT, s.NB], F16))
        iota_i = ctx.enter_context(nc.sbuf_tensor("iota_i3", [P, BANK], I32))
        iota = ctx.enter_context(nc.sbuf_tensor("iota_16", [P, BANK], F16))
        made, onehots, summed, kept = sem("made"), sem("onehots"), sem("summed"), sem("kept")
        block = ctx.enter_context(nc.Block())

        def bank(gg):
            return gg * BANK

        def group_loop(eng, group):
            for gg in range(U):
                group(0, gg)
            with eng.Fori(1, G // U) as i:
                for gg in range(U):
                    group(i, gg)
            group(G // U, 0)

        def tiles(g):
            return 1 if isinstance(g, int) and g == G else s.DT

        @block.gpsimd
        def _(pool):
            pool.iota(iota_i[:, :], pattern=[[1, BANK]], base=0, channel_multiplier=0).then_inc(made, 1)
            pool.wait_ge(made, 1)
            pool.tensor_copy(iota[:, :], iota_i[:, :]).then_inc(made, 1)
            pool.memset(lows[:, :, :, EVEN:P - 1], 0.0)
            pool.memset(lows[:, :, :, P - 1:P], 1.0).then_inc(made, 1)

        @block.vector
        def _(dve):
            def group(i, gg):
                g = U * i + gg
                dve.wait_ge(summed, g + 1)
                for j in range(tiles(g)):
                    tt = g * s.DT + j
                    dve.tensor_scalar(keys[0:s.EP, gg, j, :], iota[0:s.EP, 0:cols], k["key"][0:s.EP, bass.ds(tt, 1)],
                                      None, ALU.is_equal)
                    ins = dve.tensor_scalar(lows[0:s.EP, gg, j, 0:EVEN], iota[0:s.EP, 0:EVEN],
                                            k["low"][0:s.EP, bass.ds(tt, 1)], None, ALU.is_equal)
                if not (isinstance(g, int) and g == 0):
                    wide = [s.EP, s.DT, s.NB]
                    ins = dve.tensor_tensor(
                        nexts[0:s.EP, gg, :, :],
                        iota[0:s.EP, 0:s.NB].rearrange("p (a b) -> p a b", a=1).to_broadcast(wide),
                        k["next_key"][0:s.EP, bass.ds((g - 1) * s.DT, s.DT)].rearrange(
                            "p (j a) -> p j a", a=1).to_broadcast(wide), ALU.is_equal)
                ins.then_inc(onehots, 1)
            dve.wait_ge(made, 3)
            group_loop(dve, group)

        @block.tensor
        def _(pe):
            pe.sem_inc(summed, CREDIT)

            def group(i, gg):
                g = U * i + gg
                pe.wait_ge(kept, g + 1)
                pe.wait_ge(onehots, g + 1)
                n = tiles(g)
                alone = isinstance(g, int) and g == 0
                for j in range(n):
                    ins = pe.matmul(k["ps"][:, bank(gg):bank(gg) + cols], lows[0:s.EP, gg, j, :],
                                    keys[0:s.EP, gg, j, :], start=j == 0, stop=alone and j == n - 1)
                if not alone:
                    for j in range(s.DT):
                        ins = pe.matmul(k["ps"][:, bank(gg):bank(gg) + s.NB], lows[0:s.EP, (gg - 1) % U, j, :],
                                        nexts[0:s.EP, gg, j, :], start=False, stop=j == s.DT - 1)
                ins.then_inc(summed, 1)
            group_loop(pe, group)

        @block.scalar
        def _(act):
            act.sem_inc(kept, U)

            def group(i, gg):
                g = U * i + gg
                start = act.value_load(k["dstarts"][0:1, bass.ds(g, 1)], min_val=0, max_val=s.N - 1)
                act.wait_ge(summed, g + 1 + CREDIT)
                act.wait_ge(kept, g + U)
                act.copy(k["adj"][:, :, bass.ds(start, s.DW)],
                         k["ps"][:, bank(gg):bank(gg) + cols].rearrange("p (w b) -> p b w", b=s.NB)).then_inc(kept, 1)
            group_loop(act, group)


def dense_counts(nc, s, k, counts):
    with ExitStack() as ctx:
        sem = semaphores(nc, ctx, "dc_")
        c16 = ctx.enter_context(nc.sbuf_tensor("c16", [s.NB, s.N], F16))
        one16 = ctx.enter_context(nc.sbuf_tensor("one16", [s.NB, 1], F16))
        stored, loaded, made, done = sem("stored"), sem("loaded"), sem("made"), sem("done")
        block = ctx.enter_context(nc.Block())

        @block.sync
        def _(sp):
            sp.dma_start(counts.rearrange("(a b) n -> a b n", a=1), k["adj"][P - 1:P, :, 0:s.N]).then_inc(stored, 16)
            sp.wait_ge(stored, 16)
            sp.dma_start(c16[:, :], counts).then_inc(loaded, 16)

        @block.vector
        def _(dve):
            dve.memset(one16[:, :], 1.0).then_inc(made, 1)
            dve.wait_ge(done, 1)
            dve.tensor_scalar(k["rcnt"][0:s.NP, :], k["ps"][0:s.NP, 0:s.NB], 1.0, None, ALU.max).then_inc(made, 1)
            dve.wait_ge(made, 2)
            dve.reciprocal(k["rcnt"][0:s.NP, :], k["rcnt"][0:s.NP, :])

        @block.tensor
        def _(pe):
            pe.wait_ge(made, 1)
            pe.wait_ge(loaded, 16)
            for b in range(s.NB):
                ins = pe.matmul(k["ps"][0:s.NP, b:b + 1], c16[:, b * s.NP:(b + 1) * s.NP], one16[:, :],
                                start=True, stop=True)
            ins.then_inc(done, 1)


def count_row(nc, s, k, counts):
    with ExitStack() as ctx:
        sem = semaphores(nc, ctx, "cr_")
        c16 = ctx.enter_context(nc.sbuf_tensor("c16r", [s.NB, s.N], F16))
        one16 = ctx.enter_context(nc.sbuf_tensor("one16r", [s.NB, 1], F16))
        loaded, made, done = sem("loaded"), sem("made"), sem("done")
        block = ctx.enter_context(nc.Block())

        @block.sync
        def _(sp):
            sp.dma_start(c16[:, :], counts).then_inc(loaded, 16)

        @block.vector
        def _(dve):
            dve.memset(one16[:, :], 1.0).then_inc(made, 1)
            for c in range(s.CH):
                dve.wait_ge(done, c + 1)
                dve.tensor_copy(k["cnt1"][0:1, c * BANK:c * BANK + chunk(s, c)],
                                k["ps"][0:1, c * BANK:c * BANK + chunk(s, c)])

        @block.tensor
        def _(pe):
            pe.wait_ge(made, 1)
            pe.wait_ge(loaded, 16)
            for c in range(s.CH):
                pe.matmul(k["ps"][0:1, c * BANK:c * BANK + chunk(s, c)], one16[:, :],
                          c16[:, c * BANK:c * BANK + chunk(s, c)], start=True, stop=True).then_inc(done, 1)


def dense_layers(nc, s, k):
    per = BANK // D
    NQ = -(-s.NB // per)
    L = 3
    with ExitStack() as ctx:
        def sb(name, shape, dt=F32):
            return ctx.enter_context(nc.sbuf_tensor(name, shape, dt))
        sem = semaphores(nc, ctx, "dl_")
        parts = sb("parts", [P, 3, s.NB, D], BF16)
        root = sb("root", [P, s.NB * D])
        turn = sb("turn", [P, per * s.NP])
        rest = sb("rest", [P, BANK])
        summed, agg_kept, o_ready, h_ready, t_ready, hT_kept, r_ready, root_kept = (
            sem("summed"), sem("agg_kept"), sem("o_ready"), sem("h_ready"), sem("t_ready"), sem("hT_kept"),
            sem("r_ready"), sem("root_kept"))
        scaled, high, rest1, mid, low = sem("scaled"), sem("high"), sem("rest1"), sem("mid"), sem("low")
        block = ctx.enter_context(nc.Block())
        ps = k["ps"]
        D_BANK, O_BANK, T_BANK, R_BANK = (0, 1), 2, 3, 4

        def blocks(q):
            return min(per, s.NB - q * per)

        def rows(a, q):
            return a[0:s.NP, q * BANK:q * BANK + blocks(q) * D]

        def part(i, q):
            return parts[0:s.NP, i, q * per:q * per + blocks(q), :].rearrange("p b d -> p (b d)")

        def rest_rows(q):
            return rest[0:s.NP, 0:blocks(q) * D]

        @block.tensor
        def _(pe):
            def stage_o(l, q):
                n = (l - 1) * NQ + q
                pe.wait_ge(agg_kept, n + 1)
                if n:
                    pe.wait_ge(h_ready, n)
                for j in range(blocks(q)):
                    ins = pe.matmul(ps[0:s.NP, O_BANK * BANK + j * D:O_BANK * BANK + (j + 1) * D],
                                    turn[:, j * s.NP:(j + 1) * s.NP], k[f"W{l}l"][:, :], start=True, stop=True)
                ins.then_inc(o_ready, 1)

            def stage_t(l, q):
                n = l * NQ + q
                if l:
                    pe.wait_ge(h_ready, (l - 1) * NQ + q + 1)
                if n:
                    pe.wait_ge(hT_kept, n)
                for j in range(blocks(q)):
                    b = q * per + j
                    ins = pe.transpose(ps[:, T_BANK * BANK + j * s.NP:T_BANK * BANK + (j + 1) * s.NP],
                                       k["hn"][0:s.NP, b * D:(b + 1) * D], k["ident"][0:s.NP, 0:s.NP])
                ins.then_inc(t_ready, 1)

            def stage_r(l, q):
                n = l * NQ + q
                pe.wait_ge(hT_kept, n + 1)
                if n:
                    pe.wait_ge(root_kept, n)
                for j in range(blocks(q)):
                    o = ps[0:s.NP, R_BANK * BANK + j * D:R_BANK * BANK + (j + 1) * D]
                    pe.matmul(o, turn[:, j * s.NP:(j + 1) * s.NP], k[f"W{l + 1}r"][:, :], start=True, stop=False)
                    ins = pe.matmul(o, k["ones"][0:1, 0:s.NP], k[f"b{l + 1}"][0:1, :], start=False, stop=True)
                ins.then_inc(r_ready, 1)

            def after(l, q, stage):
                if l == 1 and q == 0:
                    return
                l, q = (l, q - 1) if q else (l - 1, NQ - 1)
                if stage == 0:
                    stage_o(l, q)
                elif l < L:
                    (stage_t if stage == 1 else stage_r)(l, q)
            for q in range(NQ):
                stage_t(0, q)
                stage_r(0, q)
            for l in range(1, L + 1):
                for q in range(NQ):
                    n = (l - 1) * NQ + q
                    width = blocks(q) * s.NP
                    if n >= 2:
                        pe.wait_ge(agg_kept, n - 1)
                    for b in range(s.NB):
                        if q == 0 and b % per == 0:
                            pe.wait_ge(low, (l - 1) * NQ + b // per + 1)
                        if b in (3, 8, 14):
                            after(l, q, (3, 8, 14).index(b))
                        for i in range(3):
                            ins = pe.matmul(ps[:, D_BANK[n % 2] * BANK:D_BANK[n % 2] * BANK + width],
                                            parts[0:s.NP, i, b, :], k["adj"][0:s.NP, b, q * per * s.NP:q * per * s.NP + width],
                                            start=b == 0 and i == 0, stop=b == s.NB - 1 and i == 2)
                    ins.then_inc(summed, 1)
            stage_o(L, NQ - 1)

        @block.scalar
        def _(act):
            def turned(l, q):
                n = l * NQ + q
                act.wait_ge(t_ready, n + 1)
                if l:
                    act.wait_ge(o_ready, (l - 1) * NQ + q + 1)
                if n:
                    act.wait_ge(r_ready, n)
                act.copy(turn[:, 0:blocks(q) * s.NP], ps[:, T_BANK * BANK:T_BANK * BANK + blocks(q) * s.NP]
                         ).then_inc(hT_kept, 1)

            def split_high(l, q):
                if l:
                    act.wait_ge(summed, l * NQ)
                    act.wait_ge(h_ready, (l - 1) * NQ + q + 1)
                act.copy(part(0, q), rows(k["hn"], q)).then_inc(high, 1)
            for q in range(NQ):
                split_high(0, q)
                turned(0, q)
            for l in range(1, L + 1):
                for q in range(NQ):
                    n = (l - 1) * NQ + q
                    act.wait_ge(summed, n + 1)
                    act.wait_ge(r_ready, l * NQ + q if l < L else L * NQ)
                    if l == L and q:
                        act.wait_ge(o_ready, n)
                    act.copy(turn[:, 0:blocks(q) * s.NP],
                             ps[:, D_BANK[n % 2] * BANK:D_BANK[n % 2] * BANK + blocks(q) * s.NP]).then_inc(agg_kept, 1)
                    if l < L:
                        if q == NQ - 1:
                            for c in range(NQ - 1):
                                split_high(l, c)
                        turned(l, q)
                        if q == NQ - 1:
                            split_high(l, q)

        @block.vector
        def _(dve):
            def keep_root(l, q):
                n = l * NQ + q
                dve.wait_ge(r_ready, n + 1)
                dve.tensor_copy(rows(root, q), ps[0:s.NP, R_BANK * BANK:R_BANK * BANK + blocks(q) * D]
                                ).then_inc(root_kept, 1)

            def split_rest(l, q):
                n = l * NQ + q
                dve.wait_ge(high, n + 1)
                if n:
                    dve.wait_ge(low, n)
                dve.tensor_tensor(rest_rows(q), rows(k["hn"], q), part(0, q), ALU.subtract).then_inc(rest1, 1)
            for q in range(NQ):
                split_rest(0, q)
                keep_root(0, q)
            count = [0]
            for l in range(1, L + 1):
                for q in range(NQ):
                    n = (l - 1) * NQ + q
                    ends = l < L and q == NQ - 1
                    if ends:
                        for c in range(2):
                            split_rest(l, c)
                    dve.wait_ge(o_ready, n + 1)
                    dve.wait_ge(root_kept, (l - 1) * NQ + q + 1)
                    for j in range(blocks(q)):
                        b = q * per + j
                        ins = dve.scalar_tensor_tensor(
                            out=k["hn"][0:s.NP, b * D:(b + 1) * D],
                            in0=ps[0:s.NP, O_BANK * BANK + j * D:O_BANK * BANK + (j + 1) * D],
                            scalar=k["rcnt"][0:s.NP, b:b + 1], in1=root[0:s.NP, b * D:(b + 1) * D],
                            op0=ALU.mult, op1=ALU.add)
                    if l == L:
                        ins.then_inc(h_ready, 1)
                        continue
                    ins.then_inc(scaled, 1)
                    count[0] += 1
                    dve.wait_ge(scaled, count[0])
                    dve.tensor_scalar(rows(k["hn"], q), rows(k["hn"], q), 0.0, None, ALU.max).then_inc(h_ready, 1)
                    if ends:
                        for c in range(2, NQ - 1):
                            split_rest(l, c)
                    keep_root(l, q)
                    if ends:
                        split_rest(l, q)

        @block.gpsimd
        def _(pool):
            for l in range(L):
                for q in range(NQ):
                    n = l * NQ + q
                    pool.wait_ge(rest1, n + 1)
                    pool.tensor_copy(part(1, q), rest_rows(q)).then_inc(mid, 1)
                    pool.wait_ge(mid, n + 1)
                    pool.tensor_tensor(part(2, q), rest_rows(q), part(1, q), ALU.subtract).then_inc(low, 1)


INPUTS = ("x", "src", "dst", "edge_attr_128", "L0_gnn_W1l", "L0_gnn_b1", "L0_gnn_W1r", "L0_gnn_W2l", "L0_gnn_b2",
          "L0_gnn_W2r", "L0_gnn_W3l", "L0_gnn_b3", "L0_gnn_W3r", "L1_gnn_We1", "L1_gnn_be1", "L1_gnn_We2",
          "L1_gnn_be2", "L1_gnn_Wu1", "L1_gnn_bu1", "L1_gnn_Wu2", "L1_gnn_bu2", "L1_gnn_eps")


def kernel(**inputs):
    import concourse.bacc as bacc
    from concourse.bass_utils import run_bass_kernel_spmd

    nc = bacc.Bacc("TRN2", target_bir_lowering=False, num_devices=1)
    arrays, t = {}, {}
    for name in INPUTS:
        a = np.ascontiguousarray(inputs[name])
        arrays["in_" + name] = a
        t[name] = nc.dram_tensor("in_" + name, a.shape, mybir.dt.from_np(a.dtype), kind="ExternalInput").ap()
    out = nc.dram_tensor("out", inputs["x"].shape, F32, kind="ExternalOutput").ap()
    gnn_kernel(nc, t, out)
    r = run_bass_kernel_spmd(nc, [arrays], core_ids=[0])
    return r.results[0]["out"]
```
